# Optimizing a Trainium2 kernel written in Bass

```python
import numpy as np
import jax
import jax.numpy as jnp

def _softmax(x, axis=-1):
    return jax.nn.softmax(x, axis=axis)

def _gelu(x):
    return jax.nn.gelu(x, approximate=True)

def _silu(x):
    return jax.nn.silu(x)

def _sigmoid(x):
    return jax.nn.sigmoid(x)

def _layernorm(x, axis=-1, eps=1e-05):
    m = jnp.mean(x, axis=axis, keepdims=True)
    v = jnp.var(x, axis=axis, keepdims=True)
    return (x - m) / jnp.sqrt(v + eps)

def _scatter_add(tgt, idx, src, axis=0):
    return tgt.at[idx].add(src)

def _segment_sum(src, seg, n):
    return jax.ops.segment_sum(src, seg, n)
kernel_name = 'mk_adj_preln_d1_adj_r2_e3f1a6'

def setup_inputs(seed: int=0):
    np.random.seed(seed)
    _w = jnp.asarray

    def _rec_inputs():
        import jax
        import jax.numpy as jnp
        _gk = jax.random.key(seed)
        x = 0.5001 + 0.2887 * jax.random.normal(jax.random.fold_in(_gk, 1), (8192, 64), jnp.float32)
        _a = jax.random.bernoulli(jax.random.fold_in(_gk, 2), 0.000244141, (8192, 8192))
        _a = jnp.logical_or(_a, jnp.eye(8192, dtype=bool))
        _af = _a.astype(jnp.float32)
        _af = _af * jax.random.uniform(jax.random.fold_in(_gk, 3), (8192, 8192), jnp.float32, 0.05, 1)
        adj = _af
        return (x, adj)
    x, adj = _rec_inputs()

    def _L0_gnn_setup():
        import jax, jax.numpy as jnp
        import numpy as np
        N = 5000
        DIM = 64
        F_CONST = 1.0
        B_CONST = 0.1
        R_CONST = 0.01
        key = jax.random.key(seed)
        k1, k2 = jax.random.split(key)
        t = jnp.zeros((1,), dtype=jnp.float32)
        x = jax.random.uniform(k1, (N, DIM), dtype=jnp.float32)
        A = jax.random.uniform(k2, (N, N), dtype=jnp.float32)
        return {'t': t, 'x': x, 'A': A}
    _L0_gnn_all = _L0_gnn_setup()
    _L0_gnn_in = {k: v for k, v in _L0_gnn_all.items() if k in ('t',)}
    del _L0_gnn_all
    return {'x': x, 'adj': adj, 'L0_gnn_t': _L0_gnn_in['t']}

def reference(x, adj, L0_gnn_t):
    import jax
    import jax.numpy as jnp

    def _L0_gnn_ref(t, x, A):
        import jax, jax.numpy as jnp
        import numpy as np
        N = 5000
        DIM = 64
        F_CONST = 1.0
        B_CONST = 0.1
        R_CONST = 0.01
        Ax = A @ x
        outer = R_CONST * jnp.sum(x * Ax, axis=1, keepdims=True)
        return F_CONST - B_CONST * x - outer
    h = jnp.maximum(_layernorm(x, axis=-1), 0.0)
    x = x + _L0_gnn_ref(L0_gnn_t, h, adj)
    return x

_drawn_inputs = setup_inputs


def setup_inputs(seed=0):
    import zlib

    import numpy as np

    out = dict(_drawn_inputs(seed))
    spreads = {}
    factors = {}
    for name, (base, spread) in spreads.items():
        noise = np.random.default_rng([zlib.crc32(name.encode()), seed]).standard_normal(out[name].shape)
        drawn = base * np.exp(spread * noise) if base else spread * noise
        out[name] = jnp.asarray(drawn.astype(out[name].dtype))
    for name, factor in factors.items():
        out[name] = (out[name] * factor).astype(out[name].dtype)
    return out
```

```python
import concourse.bass as bass
from concourse import mybir
from contextlib import ExitStack


def gnn_layer(nc: bass.Bass, x: bass.AP, adj: bass.AP, out: bass.AP):
    fp32 = mybir.dt.float32
    fp32r = mybir.dt.float32r
    i32 = mybir.dt.int32
    ALU = mybir.AluOpType
    ACT = mybir.ActivationFunctionType
    AX = mybir.AxisListType

    F_CONST, B_CONST, R_CONST, EPS = 1.0, 0.1, 0.01, 1e-5
    HI_MASK = -4096

    P = 128
    N, D = x.shape
    R = 4
    NB = N // (P * R)
    HALVES = 2
    HC = N // HALVES
    GC = 2048
    BANK = 512
    GB = GC // BANK
    BANKS = 2 * GB
    NG = N // GC
    GPB = NG * R
    NQ = 8
    QB = NB // NQ
    QT = QB * R

    x_v = x.rearrange("(b p r) d -> p b (r d)", p=P, r=R)
    out_v = out.rearrange("(b p r) d -> p b (r d)", p=P, r=R)
    adj_v = adj.rearrange("(b p r) (h c) -> b r h p c", p=P, r=R, h=HALVES)

    ctx = ExitStack()
    with ctx:
        def sb(name, shape, dt):
            return ctx.enter_context(nc.sbuf_tensor(name, shape, dt))

        def sem(name):
            return ctx.enter_context(nc.semaphore(name))

        adj_rows = sb("adj_rows", [P, R, HALVES, HC], fp32)
        hT = sb("hT", [P, N], fp32r)
        weights = sb("weights", [P, 2, 2, P], fp32r)
        base = sb("base", [P, NB, R * D], fp32)
        xc = sb("xc", [P, 2, QT, D], fp32)
        sq = sb("sq", [P, QT, D], fp32)
        hilo = sb("hilo", [P, 2, QT, 2, D], fp32)
        decay = sb("decay", [P, QT, D], fp32)
        mean = sb("mean", [P, NQ, QT], fp32)
        var = sb("var", [P, NQ, QT], fp32)
        std = sb("std", [P, NQ, QT], fp32)
        rstd = sb("rstd", [P, NQ, QT], fp32)
        newton = sb("newton", [P, NQ, QT], fp32)
        ident = sb("ident", [P, P], fp32)
        partial = sb("partial", [P, NB, R, NG], fp32)
        psum_row = sb("psum_row", [P, NG], fp32)
        outer = sb("outer", [P, R], fp32)
        gram = ctx.enter_context(nc.psum_tensor("gram", [P, 2, GC], fp32))

        def bank(n):
            return gram[:, n // GB, n % GB * BANK:(n % GB + 1) * BANK]

        x_loaded = [sem(f"x_loaded{q}") for q in range(NQ)]
        adj_loaded = [[sem(f"adj_loaded{r}_{h}") for h in range(HALVES)] for r in range(R)]
        ident_zeroed = sem("ident_zeroed")
        ident_ready = sem("ident_ready")
        dve_step = sem("dve_step")
        centred = sem("centred")
        squared = sem("squared")
        variance = sem("variance")
        std_ready = sem("std_ready")
        h_ready = sem("h_ready")
        split = sem("split")
        decay_ready = sem("decay_ready")
        base_ready = sem("base_ready")
        transposed = sem("transposed")
        hT_ready = sem("hT_ready")
        weights_ready = sem("weights_ready")
        gram_ready = sem("gram_ready")
        gram_used = sem("gram_used")
        outer_ready = sem("outer_ready")
        out_ready = sem("out_ready")
        stored = sem("stored")

        block = ctx.enter_context(nc.Block())

        @block.sync
        def _(sp):
            for q in range(NQ):
                sp.dma_start(base[:, q * QB:(q + 1) * QB, :], x_v[:, q * QB:(q + 1) * QB, :]).then_inc(x_loaded[q], 16)
            for r in range(R):
                for h in range(HALVES):
                    sp.dma_start(adj_rows[:, r, h, :], adj_v[0, r, h, :, :]).then_inc(adj_loaded[r][h], 16)
            with sp.Fori(1, NB) as b:
                for r in range(R):
                    for h in range(HALVES):
                        sp.wait_ge(gram_used, (b - 1) * GPB + (r * NG + (h + 1) * (HC // GC) + 2))
                        sp.dma_start(adj_rows[:, r, h, :], adj_v[b, r, h, :, :]).then_inc(adj_loaded[r][h], 16)

        @block.gpsimd
        def _(pool):
            nc.gpsimd.memset(ident[:, :], 0.0).then_inc(ident_zeroed, 1)
            pool.wait_ge(ident_zeroed, 1)
            nc.gpsimd.affine_select(out=ident[:, :], in_=ident[:, :], compare_op=ALU.not_equal, fill=1.0, base=0,
                                    pattern=[[-1, P]], channel_multiplier=1).then_inc(ident_ready, 1)
            for q in range(NQ):
                pool.wait_ge(h_ready, q + 1)
                if q >= 1:
                    pool.wait_ge(base_ready, q)
                nc.gpsimd.tensor_scalar(decay[:, :, :], xc[:, q % 2, :, :], -B_CONST, F_CONST,
                                        ALU.mult, ALU.add).then_inc(decay_ready, 1)
                pool.wait_ge(decay_ready, q + 1)
                b_q = base[:, q * QB:(q + 1) * QB, :].rearrange("p b (r d) -> p (b r) d", r=R)
                nc.gpsimd.tensor_tensor(b_q, b_q, decay[:, :, :], ALU.add).then_inc(base_ready, 1)

        @block.vector
        def _(dve):
            steps = [0]

            def chain(ins):
                steps[0] += 1
                ins.then_inc(dve_step, 1)
                dve.wait_ge(dve_step, steps[0])

            def centre(q):
                x_q = base[:, q * QB:(q + 1) * QB, :].rearrange("p b (r d) -> p (b r) d", r=R)
                dve.wait_ge(x_loaded[q], 16)
                chain(nc.vector.reduce_sum(mean[:, q, :], x_q, AX.X))
                chain(nc.vector.tensor_scalar(mean[:, q, :], mean[:, q, :], 1.0 / D, None, ALU.mult))
                if q >= 2:
                    dve.wait_ge(decay_ready, q - 1)
                nc.vector.tensor_tensor(xc[:, q % 2, :, :], x_q, mean[:, q, :].unsqueeze(2).to_broadcast([P, QT, D]),
                                        ALU.subtract).then_inc(centred, 1)

            def normalise(q):
                dve.wait_ge(squared, q + 1)
                chain(nc.vector.reduce_sum(var[:, q, :], sq[:, :, :], AX.X))
                nc.vector.tensor_scalar(var[:, q, :], var[:, q, :], 1.0 / D, EPS, ALU.mult, ALU.add).then_inc(variance, 1)
                dve.wait_ge(std_ready, q + 1)
                chain(nc.vector.reciprocal(rstd[:, q, :], std[:, q, :]))
                chain(nc.vector.tensor_tensor(newton[:, q, :], rstd[:, q, :], rstd[:, q, :], ALU.mult))
                chain(nc.vector.tensor_tensor(newton[:, q, :], newton[:, q, :], var[:, q, :], ALU.mult))
                chain(nc.vector.tensor_scalar(newton[:, q, :], newton[:, q, :], -0.5, 1.5, ALU.mult, ALU.add))
                chain(nc.vector.tensor_tensor(rstd[:, q, :], rstd[:, q, :], newton[:, q, :], ALU.mult))
                h_q = xc[:, q % 2, :, :]
                dve.wait_ge(squared, q + 1)
                nc.vector.scalar_tensor_tensor(out=h_q, in0=h_q, scalar=0.0,
                                               in1=rstd[:, q, :].unsqueeze(2).to_broadcast([P, QT, D]),
                                               op0=ALU.max, op1=ALU.mult).then_inc(h_ready, 1)
                dve.wait_ge(h_ready, q + 1)
                if q >= 2:
                    dve.wait_ge(transposed, QB * (q - 1))
                chain(nc.vector.tensor_single_scalar(hilo[:, q % 2, :, 0, :].bitcast(i32), h_q.bitcast(i32), HI_MASK,
                                                     ALU.bitwise_and))
                nc.vector.tensor_tensor(hilo[:, q % 2, :, 1, :], h_q, hilo[:, q % 2, :, 0, :],
                                        ALU.subtract).then_inc(split, 1)

            centre(0)
            for q in range(NQ):
                if q + 1 < NQ:
                    centre(q + 1)
                normalise(q)

            with dve.Fori(0, NB) as b:
                for r in range(R):
                    for g in range(NG):
                        h, c = divmod(g * GC, HC)
                        if c == 0:
                            dve.wait_ge(adj_loaded[r][h], b * 16 + 16)
                        dve.wait_ge(gram_ready, b * GPB + (r * NG + g + 1))
                        a = adj_rows[:, r, h, c:c + GC]
                        nc.vector.scalar_tensor_tensor(out=a, in0=a, scalar=1.0, in1=gram[:, g % 2, :],
                                                       op0=ALU.mult, op1=ALU.mult,
                                                       accum_out=partial[:, b, r, g:g + 1]).then_inc(gram_used, 1)

        @block.tensor
        def _(pe):
            pe.wait_ge(ident_ready, 1)
            for q in range(NQ):
                pe.wait_ge(split, q + 1)
                for k in range(QB):
                    n = q * QB + k
                    if n >= BANKS:
                        pe.wait_ge(hT_ready, n - BANKS + 1)
                    for r in range(R):
                        ins = nc.tensor.transpose(bank(n % BANKS)[:, r * P:(r + 1) * P],
                                                  hilo[:, q % 2, k * R + r, :, :].rearrange("p s d -> p (s d)"), ident[:, :])
                    ins.then_inc(transposed, 1)
            pe.wait_ge(hT_ready, NB - 2)
            pe.wait_ge(gram_used, 2)
            with pe.Fori(0, NB) as b:
                for r in range(R):
                    pe.wait_ge(weights_ready, b * R + (r + 1))
                    for g in range(NG):
                        pe.wait_ge(gram_used, b * GPB + (r * NG + g + 1))
                        for s in range(2):
                            for k in range(GB):
                                c = g * GC + k * BANK
                                ins = nc.tensor.matmul(gram[:, g % 2, k * BANK:(k + 1) * BANK], weights[:, r % 2, s, :],
                                                       hT[:, c:c + BANK], start=(s == 0), stop=(s == 1))
                        ins.then_inc(gram_ready, 1)

        @block.scalar
        def _(act):
            def spread(q):
                act.wait_ge(centred, q + 1)
                if q >= 1:
                    act.wait_ge(variance, q)
                nc.scalar.activation(sq[:, :, :], xc[:, q % 2, :, :], ACT.Square).then_inc(squared, 1)

            def take_hT(q):
                for k in range(QB):
                    n = q * QB + k
                    act.wait_ge(transposed, n + 1)
                    src = bank(n % BANKS).rearrange("k (r p) -> k p r", r=R)
                    dst = hT[:, n * BANK:(n + 1) * BANK].rearrange("k (p r) -> k p r", r=R)
                    ins = nc.scalar.copy(dst, src)
                    ins.then_inc(hT_ready if n < NB - 2 else gram_used, 1)

            spread(0)
            for q in range(NQ):
                if q + 1 < NQ:
                    spread(q + 1)
                act.wait_ge(variance, q + 1)
                nc.scalar.activation(std[:, q, :], var[:, q, :], ACT.Sqrt).then_inc(std_ready, 1)
                if q >= 1:
                    take_hT(q - 1)
            take_hT(NQ - 1)

            def lay_weights(b, r):
                rows = hT[:, :].rearrange("k (b p r) -> k b r p", r=R, p=P)
                nc.scalar.copy(weights[:, r % 2, 0, :], rows[:, b, r, :])
                nc.scalar.copy(weights[0:D, r % 2, 1, :], rows[D:2 * D, b, r, :])
                nc.scalar.copy(weights[D:2 * D, r % 2, 1, :], rows[0:D, b, r, :]).then_inc(weights_ready, 1)

            def finish(b, r):
                act.wait_ge(gram_used, b * GPB + ((r + 1) * NG + 2))
                nc.scalar.activation(psum_row[:, :], partial[:, b, r, :], ACT.Copy, scale=-R_CONST,
                                     accum_out=outer[:, r:r + 1]).then_inc(outer_ready, 1)
                act.wait_ge(outer_ready, b * R + (r + 1))
                y = base[:, b, r * D:(r + 1) * D]
                nc.scalar.activation(y, y, ACT.Identity, bias=outer[:, r:r + 1]).then_inc(out_ready, 1)

            def store(b):
                act.wait_ge(out_ready, b * R + R)
                act.dma_start(out_v[:, b, :], base[:, b, :]).then_inc(stored, 16)

            act.wait_ge(hT_ready, NB - 2)
            act.wait_ge(gram_used, 2)
            act.wait_ge(base_ready, NQ)
            for r in range(R):
                if r >= 2:
                    act.wait_ge(gram_ready, (r - 1) * NG)
                lay_weights(0, r)
                if r >= 2:
                    finish(0, r - 2)
            with act.Fori(1, NB) as b:
                for r in range(R):
                    act.wait_ge(gram_ready, b * GPB + (r - 1) * NG)
                    lay_weights(b, r)
                    if r < 2:
                        finish(b - 1, r + 2)
                    else:
                        finish(b, r - 2)
                    if r == 1:
                        store(b - 1)
            finish(NB - 1, 2)
            finish(NB - 1, 3)
            store(NB - 1)
            act.wait_ge(stored, 16 * NB)


def kernel(x, adj, L0_gnn_t):
    import numpy as np
    import concourse.bacc as bacc
    from concourse.bass_utils import run_bass_kernel_spmd

    nc = bacc.Bacc("TRN2", target_bir_lowering=False, num_devices=1)
    arrays = {"x": np.ascontiguousarray(x), "adj": np.ascontiguousarray(adj)}
    ins = [nc.dram_tensor(name, a.shape, mybir.dt.from_np(a.dtype), kind="ExternalInput").ap()
           for name, a in arrays.items()]
    out = nc.dram_tensor("out", arrays["x"].shape, mybir.dt.float32, kind="ExternalOutput").ap()
    gnn_layer(nc, *ins, out)
    result = run_bass_kernel_spmd(nc, [arrays], core_ids=[0])
    return result.results[0]["out"]
```

```python
import concourse.bass as bass
from concourse import mybir
from contextlib import ExitStack


def gnn_layer(nc: bass.Bass, x: bass.AP, adj: bass.AP, out: bass.AP):
    fp32 = mybir.dt.float32
    fp32r = mybir.dt.float32r
    i32 = mybir.dt.int32
    ALU = mybir.AluOpType
    ACT = mybir.ActivationFunctionType
    AX = mybir.AxisListType

    F_CONST, B_CONST, R_CONST, EPS = 1.0, 0.1, 0.01, 1e-5
    HI_MASK = -4096

    P = 128
    N, D = x.shape
    R = 4
    NB = N // (P * R)
    HALVES = 2
    HC = N // HALVES
    GC = 2048
    BANK = 512
    GB = GC // BANK
    NG = N // GC
    GPB = NG * R
    LAST = [(g * GC, GC) for g in range(NG - 1)] + [(N - GC, GC // 2), (N - GC // 2, GC // 2)]
    NQ = 4
    QB = NB // NQ
    QT = QB * R
    PARTS = 2
    PB = QB // PARTS
    PT = PB * R

    x_v = x.rearrange("(b p r) d -> p b (r d)", p=P, r=R)
    out_v = out.rearrange("(b p r) d -> p b (r d)", p=P, r=R)
    adj_v = adj.rearrange("(b p r) c -> b r p c", p=P, r=R)

    ctx = ExitStack()
    with ctx:
        def sb(name, shape, dt):
            return ctx.enter_context(nc.sbuf_tensor(name, shape, dt))

        def sem(name):
            return ctx.enter_context(nc.semaphore(name))

        adj_rows = sb("adj_rows", [P, R, N], fp32)
        hT = sb("hT", [P, N], fp32r)
        weights = sb("weights", [P, 2, 2, P], fp32r)
        base = sb("base", [P, NB, R * D], fp32)
        h = sb("h", [P, NQ, QT, D], fp32)
        hilo = sb("hilo", [P, 2, PT, 2, D], fp32)
        total = sb("total", [P, NQ, QT], fp32)
        half_var = sb("half_var", [P, NQ, QT], fp32)
        std = sb("std", [P, NQ, QT], fp32)
        rstd = sb("rstd", [P, NQ, QT], fp32)
        newton = sb("newton", [P, NQ, QT], fp32)
        ident = sb("ident", [P, P], fp32)
        partial = sb("partial", [P, NB, R, len(LAST)], fp32)
        unread = sb("unread", [P, len(LAST)], fp32)
        outer = sb("outer", [P, R], fp32)
        gram = ctx.enter_context(nc.psum_tensor("gram", [P, 2, GC], fp32))

        def bank(n):
            return gram[:, 0, n % GB * BANK:(n % GB + 1) * BANK]

        def sq(q):
            return gram[:, 1, q % 2 * QT * D:(q % 2 + 1) * QT * D].rearrange("p (t d) -> p t d", d=D)

        x_loaded = [sem(f"x_loaded{q}") for q in range(NQ)]
        adj_loaded = [[sem(f"adj_loaded{r}_{h}") for h in range(HALVES)] for r in range(R)]
        last_loaded = [sem(f"last_loaded{i}") for i in range(len(LAST))]
        ident_zeroed = sem("ident_zeroed")
        ident_ready = sem("ident_ready")
        dve_step = sem("dve_step")
        centred = sem("centred")
        squared = sem("squared")
        variance = sem("variance")
        std_ready = sem("std_ready")
        split = sem("split")
        decay_ready = sem("decay_ready")
        base_ready = sem("base_ready")
        transposed = sem("transposed")
        hT_ready = sem("hT_ready")
        weights_ready = sem("weights_ready")
        gram_ready = sem("gram_ready")
        gram_used = sem("gram_used")
        outer_ready = sem("outer_ready")
        out_ready = sem("out_ready")
        stored = sem("stored")

        block = ctx.enter_context(nc.Block())

        @block.sync
        def _(sp):
            def load(b, r, half):
                sp.dma_start(adj_rows[:, r, half * HC:(half + 1) * HC],
                             adj_v[b, r, :, half * HC:(half + 1) * HC]).then_inc(adj_loaded[r][half], 16)

            def slot_free(b, r, half):
                sp.wait_ge(gram_used, (b - 1) * GPB + (r * NG + (half + 1) * (HC // GC) + 2))

            for q in range(NQ):
                sp.dma_start(base[:, q * QB:(q + 1) * QB, :], x_v[:, q * QB:(q + 1) * QB, :]).then_inc(x_loaded[q], 16)
            for r in range(R):
                for half in range(HALVES):
                    load(0, r, half)
            with sp.Fori(1, NB - 1) as b:
                for r in range(R):
                    for half in range(HALVES):
                        slot_free(b, r, half)
                        load(b, r, half)
            for r in range(R - 1):
                for half in range(HALVES):
                    slot_free(NB - 1, r, half)
                    load(NB - 1, r, half)
            for i, (c, w) in enumerate(LAST):
                if c % HC == 0:
                    slot_free(NB - 1, R - 1, c // HC)
                sp.dma_start(adj_rows[:, R - 1, c:c + w],
                             adj_v[NB - 1, R - 1, :, c:c + w]).then_inc(last_loaded[i], 16)

        @block.gpsimd
        def _(pool):
            nc.gpsimd.memset(ident[:, :], 0.0).then_inc(ident_zeroed, 1)
            pool.wait_ge(ident_zeroed, 1)
            nc.gpsimd.affine_select(out=ident[:, :], in_=ident[:, :], compare_op=ALU.not_equal, fill=1.0, base=0,
                                    pattern=[[-1, P]], channel_multiplier=1).then_inc(ident_ready, 1)
            pool.wait_ge(split, PARTS * NQ)
            for q in range(NQ):
                nc.gpsimd.tensor_scalar(h[:, q, :, :], h[:, q, :, :], -B_CONST, F_CONST,
                                        ALU.mult, ALU.add).then_inc(decay_ready, 1)
                pool.wait_ge(decay_ready, q + 1)
                b_q = base[:, q * QB:(q + 1) * QB, :].rearrange("p b (r d) -> p (b r) d", r=R)
                nc.gpsimd.tensor_tensor(b_q, b_q, h[:, q, :, :], ALU.add).then_inc(base_ready, 1)

        @block.vector
        def _(dve):
            steps = [0]

            def chain(ins):
                steps[0] += 1
                ins.then_inc(dve_step, 1)
                dve.wait_ge(dve_step, steps[0])

            def over_features(a):
                return a.unsqueeze(2).to_broadcast([P, QT, D])

            def centre(q):
                x_q = base[:, q * QB:(q + 1) * QB, :].rearrange("p b (r d) -> p (b r) d", r=R)
                dve.wait_ge(x_loaded[q], 16)
                chain(nc.vector.reduce_sum(total[:, q, :], x_q, AX.X))
                nc.vector.scalar_tensor_tensor(out=h[:, q, :, :], in0=over_features(total[:, q, :]), scalar=1.0 / D,
                                               in1=x_q, op0=ALU.mult, op1=ALU.subtract).then_inc(centred, 1)

            def half_variance(q):
                dve.wait_ge(squared, q + 1)
                chain(nc.vector.reduce_sum(half_var[:, q, :], sq(q), AX.X))
                nc.vector.tensor_scalar(half_var[:, q, :], half_var[:, q, :], 0.5 / D, 0.5 * EPS,
                                        ALU.mult, ALU.add).then_inc(variance, 1)

            def normalise(q):
                dve.wait_ge(std_ready, q + 1)
                y, t = rstd[:, q, :], newton[:, q, :]
                chain(nc.vector.reciprocal(y, std[:, q, :]))
                chain(nc.vector.tensor_tensor(t, y, y, ALU.mult))
                chain(nc.vector.tensor_tensor(t, t, half_var[:, q, :], ALU.mult))
                chain(nc.vector.scalar_tensor_tensor(out=t, in0=t, scalar=1.5, in1=y, op0=ALU.subtract, op1=ALU.mult))
                chain(nc.vector.scalar_tensor_tensor(out=h[:, q, :, :], in0=h[:, q, :, :], scalar=0.0,
                                                     in1=over_features(t), op0=ALU.min, op1=ALU.mult))
                for k in range(PARTS):
                    part = q * PARTS + k
                    if part >= 2:
                        dve.wait_ge(transposed, PB * (part - 1))
                    h_k = h[:, q, k * PT:(k + 1) * PT, :]
                    hi = hilo[:, part % 2, :, 0, :]
                    lo = hilo[:, part % 2, :, 1, :]
                    chain(nc.vector.tensor_single_scalar(hi.bitcast(i32), h_k.bitcast(i32), HI_MASK, ALU.bitwise_and))
                    nc.vector.tensor_tensor(lo, h_k, hi, ALU.subtract).then_inc(split, 1)

            centre(0)
            centre(1)
            half_variance(0)
            for q in range(NQ):
                if q + 2 < NQ:
                    centre(q + 2)
                if q + 1 < NQ:
                    half_variance(q + 1)
                normalise(q)

            def sum_columns(b, r, c, w, piece):
                a = adj_rows[:, r, c:c + w]
                return nc.vector.scalar_tensor_tensor(out=a, in0=a, scalar=1.0,
                                                      in1=gram[:, c // GC % 2, c % GC:c % GC + w],
                                                      op0=ALU.mult, op1=ALU.mult,
                                                      accum_out=partial[:, b, r, piece:piece + 1])

            def sum_row_tile(b, r):
                for g in range(NG):
                    if g * GC % HC == 0:
                        dve.wait_ge(adj_loaded[r][g * GC // HC], b * 16 + 16)
                    dve.wait_ge(gram_ready, b * GPB + (r * NG + g + 1))
                    sum_columns(b, r, g * GC, GC, g).then_inc(gram_used, 1)

            with dve.Fori(0, NB - 1) as b:
                for r in range(R):
                    sum_row_tile(b, r)
            for r in range(R - 1):
                sum_row_tile(NB - 1, r)
            for i, (c, w) in enumerate(LAST):
                dve.wait_ge(last_loaded[i], 16)
                dve.wait_ge(gram_ready, (NB - 1) * GPB + (R - 1) * NG + c // GC + 1)
                sum_columns(NB - 1, R - 1, c, w, i).then_inc(gram_used, 1)

        @block.tensor
        def _(pe):
            pe.wait_ge(ident_ready, 1)
            for q in range(NQ):
                for k in range(QB):
                    n = q * QB + k
                    if k % PB == 0:
                        pe.wait_ge(split, n // PB + 1)
                    if n >= GB:
                        pe.wait_ge(hT_ready, n - GB + 1)
                    for r in range(R):
                        rows = hilo[:, n // PB % 2, n % PB * R + r, :, :].rearrange("p s d -> p (s d)")
                        ins = nc.tensor.transpose(bank(n)[:, r * P:(r + 1) * P], rows, ident[:, :])
                    ins.then_inc(transposed, 1)
            pe.wait_ge(hT_ready, NB - 2)
            pe.wait_ge(gram_used, 2)
            with pe.Fori(0, NB) as b:
                for r in range(R):
                    pe.wait_ge(weights_ready, b * R + (r + 1))
                    for g in range(NG):
                        pe.wait_ge(gram_used, b * GPB + (r * NG + g + 1))
                        for s in range(2):
                            for k in range(GB):
                                c = g * GC + k * BANK
                                ins = nc.tensor.matmul(gram[:, g % 2, k * BANK:(k + 1) * BANK], weights[:, r % 2, s, :],
                                                       hT[:, c:c + BANK], start=(s == 0), stop=(s == 1))
                        ins.then_inc(gram_ready, 1)

        @block.scalar
        def _(act):
            def square(q):
                act.wait_ge(centred, q + 1)
                if q >= 2:
                    act.wait_ge(variance, q - 1)
                nc.scalar.activation(sq(q), h[:, q, :, :], ACT.Square).then_inc(squared, 1)

            def take_hT(q):
                for k in range(QB):
                    n = q * QB + k
                    act.wait_ge(transposed, n + 1)
                    src = bank(n).rearrange("k (r p) -> k p r", r=R)
                    dst = hT[:, n * BANK:(n + 1) * BANK].rearrange("k (p r) -> k p r", r=R)
                    ins = nc.scalar.copy(dst, src)
                    ins.then_inc(hT_ready if n < NB - 2 else gram_used, 1)

            square(0)
            square(1)
            for q in range(NQ):
                act.wait_ge(variance, q + 1)
                nc.scalar.activation(std[:, q, :], half_var[:, q, :], ACT.Sqrt, scale=2.0).then_inc(std_ready, 1)
                if q + 2 < NQ:
                    square(q + 2)
                if q >= 1:
                    take_hT(q - 1)
            take_hT(NQ - 1)

            def lay_weights(b, r):
                rows = hT[:, :].rearrange("k (b p r) -> k b r p", r=R, p=P)
                nc.scalar.copy(weights[:, r % 2, 0, :], rows[:, b, r, :])
                nc.scalar.copy(weights[0:D, r % 2, 1, :], rows[D:2 * D, b, r, :])
                nc.scalar.copy(weights[D:2 * D, r % 2, 1, :], rows[0:D, b, r, :]).then_inc(weights_ready, 1)

            def finish(b, r, pieces=NG):
                act.wait_ge(gram_used, b * GPB + (r * NG + pieces + 2))
                nc.scalar.activation(unread[:, 0:pieces], partial[:, b, r, 0:pieces], ACT.Copy, scale=-R_CONST,
                                     accum_out=outer[:, r:r + 1]).then_inc(outer_ready, 1)
                act.wait_ge(outer_ready, b * R + (r + 1))
                y = base[:, b, r * D:(r + 1) * D]
                nc.scalar.activation(y, y, ACT.Identity, bias=outer[:, r:r + 1]).then_inc(out_ready, 1)

            def store(b):
                act.wait_ge(out_ready, b * R + R)
                act.dma_start(out_v[:, b, :], base[:, b, :]).then_inc(stored, 16)

            act.wait_ge(hT_ready, NB - 2)
            act.wait_ge(gram_used, 2)
            for r in range(R):
                if r >= 2:
                    act.wait_ge(gram_ready, (r - 1) * NG)
                lay_weights(0, r)
                if r == 2:
                    act.wait_ge(base_ready, NQ)
                if r >= 2:
                    finish(0, r - 2)
            with act.Fori(1, NB) as b:
                for r in range(R):
                    act.wait_ge(gram_ready, b * GPB + (r - 1) * NG)
                    lay_weights(b, r)
                    if r < 2:
                        finish(b - 1, r + 2)
                    else:
                        finish(b, r - 2)
                    if r == 1:
                        store(b - 1)
            finish(NB - 1, 2)
            finish(NB - 1, 3, pieces=len(LAST))
            store(NB - 1)
            act.wait_ge(stored, 16 * NB)


def kernel(x, adj, L0_gnn_t):
    import numpy as np
    import concourse.bacc as bacc
    from concourse.bass_utils import run_bass_kernel_spmd

    nc = bacc.Bacc("TRN2", target_bir_lowering=False, num_devices=1)
    arrays = {"x": np.ascontiguousarray(x), "adj": np.ascontiguousarray(adj)}
    ins = [nc.dram_tensor(name, a.shape, mybir.dt.from_np(a.dtype), kind="ExternalInput").ap()
           for name, a in arrays.items()]
    out = nc.dram_tensor("out", arrays["x"].shape, mybir.dt.float32, kind="ExternalOutput").ap()
    gnn_layer(nc, *ins, out)
    result = run_bass_kernel_spmd(nc, [arrays], core_ids=[0])
    return result.results[0]["out"]
```

```python
import concourse.bass as bass
from concourse import mybir
from contextlib import ExitStack


def gnn_layer(nc: bass.Bass, x: bass.AP, adj: bass.AP, out: bass.AP):
    fp32 = mybir.dt.float32
    fp32r = mybir.dt.float32r
    i32 = mybir.dt.int32
    ALU = mybir.AluOpType
    ACT = mybir.ActivationFunctionType
    AX = mybir.AxisListType

    F_CONST, B_CONST, R_CONST, EPS = 1.0, 0.1, 0.01, 1e-5
    HI_MASK = -4096

    P = 128
    N, D = x.shape
    R = 4
    NB = N // (P * R)
    HALVES = 2
    HC = N // HALVES
    GC = 2048
    BANK = 512
    GB = GC // BANK
    NG = N // GC
    GPB = NG * R
    LAST = [(g * GC, GC) for g in range(NG - 1)] + [(N - GC, GC // 2), (N - GC // 2, GC // 4), (N - GC // 4, GC // 4)]
    NQ = 4
    QB = NB // NQ
    QT = QB * R
    PARTS = 2
    PB = QB // PARTS
    PT = PB * R

    x_v = x.rearrange("(b p r) d -> p b (r d)", p=P, r=R)
    out_v = out.rearrange("(b p r) d -> p b (r d)", p=P, r=R)
    adj_v = adj.rearrange("(b p r) c -> b r p c", p=P, r=R)

    ctx = ExitStack()
    with ctx:
        def sb(name, shape, dt):
            return ctx.enter_context(nc.sbuf_tensor(name, shape, dt))

        def sem(name):
            return ctx.enter_context(nc.semaphore(name))

        adj_rows = sb("adj_rows", [P, R, N], fp32)
        hT = sb("hT", [P, N], fp32r)
        weights = sb("weights", [P, 2, 2, P], fp32r)
        base = sb("base", [P, NB, R * D], fp32)
        h = sb("h", [P, NQ, QT, D], fp32)
        hilo = sb("hilo", [P, 2, PT, 2, D], fp32)
        total = sb("total", [P, NQ, QT], fp32)
        half_var = sb("half_var", [P, NQ, QT], fp32)
        std = sb("std", [P, NQ, QT], fp32)
        rstd = sb("rstd", [P, NQ, QT], fp32)
        newton = sb("newton", [P, NQ, QT], fp32)
        ident = sb("ident", [P, P], fp32)
        partial = sb("partial", [P, NB, R, len(LAST)], fp32)
        unread = sb("unread", [P, len(LAST)], fp32)
        outer = sb("outer", [P, R], fp32)
        gram = ctx.enter_context(nc.psum_tensor("gram", [P, 2, GC], fp32))

        def bank(n):
            return gram[:, 1, n % GB * BANK:(n % GB + 1) * BANK]

        def sq(q):
            return gram[:, 0, q % 2 * QT * D:(q % 2 + 1) * QT * D].rearrange("p (t d) -> p t d", d=D)

        x_loaded = [sem(f"x_loaded{q}") for q in range(NQ)]
        adj_loaded = [[sem(f"adj_loaded{r}_{h}") for h in range(HALVES)] for r in range(R)]
        last_loaded = [sem(f"last_loaded{i}") for i in range(len(LAST))]
        ident_zeroed = sem("ident_zeroed")
        ident_ready = sem("ident_ready")
        dve_step = sem("dve_step")
        centred = sem("centred")
        squared = sem("squared")
        variance = sem("variance")
        std_ready = sem("std_ready")
        split = sem("split")
        decay_ready = sem("decay_ready")
        base_ready = sem("base_ready")
        transposed = sem("transposed")
        hT_ready = sem("hT_ready")
        weights_ready = sem("weights_ready")
        gram_ready = sem("gram_ready")
        gram_used = sem("gram_used")
        outer_ready = sem("outer_ready")
        out_ready = sem("out_ready")
        last_ready = sem("last_ready")
        stored = sem("stored")

        block = ctx.enter_context(nc.Block())

        @block.sync
        def _(sp):
            def load(b, r, half):
                sp.dma_start(adj_rows[:, r, half * HC:(half + 1) * HC],
                             adj_v[b, r, :, half * HC:(half + 1) * HC]).then_inc(adj_loaded[r][half], 16)

            def slot_free(b, r, half):
                sp.wait_ge(gram_used, (b - 1) * GPB + (r * NG + (half + 1) * (HC // GC) + 1))

            for q in range(NQ):
                sp.dma_start(base[:, q * QB:(q + 1) * QB, :], x_v[:, q * QB:(q + 1) * QB, :]).then_inc(x_loaded[q], 16)
            for r in range(R):
                for half in range(HALVES):
                    load(0, r, half)
            with sp.Fori(1, NB - 1) as b:
                for r in range(R):
                    for half in range(HALVES):
                        slot_free(b, r, half)
                        load(b, r, half)
            for r in range(R - 1):
                for half in range(HALVES):
                    slot_free(NB - 1, r, half)
                    load(NB - 1, r, half)
            for i, (c, w) in enumerate(LAST):
                if c % HC == 0:
                    slot_free(NB - 1, R - 1, c // HC)
                sp.dma_start(adj_rows[:, R - 1, c:c + w],
                             adj_v[NB - 1, R - 1, :, c:c + w]).then_inc(last_loaded[i], 16)

        @block.gpsimd
        def _(pool):
            nc.gpsimd.memset(ident[:, :], 0.0).then_inc(ident_zeroed, 1)
            pool.wait_ge(ident_zeroed, 1)
            nc.gpsimd.affine_select(out=ident[:, :], in_=ident[:, :], compare_op=ALU.not_equal, fill=1.0, base=0,
                                    pattern=[[-1, P]], channel_multiplier=1).then_inc(ident_ready, 1)
            pool.wait_ge(split, PARTS * NQ)
            for q in range(NQ):
                nc.gpsimd.tensor_scalar(h[:, q, :, :], h[:, q, :, :], -B_CONST, F_CONST,
                                        ALU.mult, ALU.add).then_inc(decay_ready, 1)
                pool.wait_ge(decay_ready, q + 1)
                b_q = base[:, q * QB:(q + 1) * QB, :].rearrange("p b (r d) -> p (b r) d", r=R)
                nc.gpsimd.tensor_tensor(b_q, b_q, h[:, q, :, :], ALU.add).then_inc(base_ready, 1)

        @block.vector
        def _(dve):
            steps = [0]

            def chain(ins):
                steps[0] += 1
                ins.then_inc(dve_step, 1)
                dve.wait_ge(dve_step, steps[0])

            def over_features(a):
                return a.unsqueeze(2).to_broadcast([P, QT, D])

            def centre(q):
                x_q = base[:, q * QB:(q + 1) * QB, :].rearrange("p b (r d) -> p (b r) d", r=R)
                dve.wait_ge(x_loaded[q], 16)
                chain(nc.vector.reduce_sum(total[:, q, :], x_q, AX.X))
                nc.vector.scalar_tensor_tensor(out=h[:, q, :, :], in0=over_features(total[:, q, :]), scalar=1.0 / D,
                                               in1=x_q, op0=ALU.mult, op1=ALU.subtract).then_inc(centred, 1)

            def half_variance(q):
                dve.wait_ge(squared, q + 1)
                summing = nc.vector.reduce_sum(half_var[:, q, :], sq(q), AX.X)
                if q < NQ - 1:
                    chain(summing)
                else:
                    summing.then_inc(gram_used, 1)
                    dve.wait_ge(gram_used, 1)
                nc.vector.tensor_scalar(half_var[:, q, :], half_var[:, q, :], 0.5 / D, 0.5 * EPS,
                                        ALU.mult, ALU.add).then_inc(variance, 1)

            def normalise(q):
                dve.wait_ge(std_ready, q + 1)
                y, t = rstd[:, q, :], newton[:, q, :]
                chain(nc.vector.reciprocal(y, std[:, q, :]))
                chain(nc.vector.tensor_tensor(t, y, y, ALU.mult))
                chain(nc.vector.tensor_tensor(t, t, half_var[:, q, :], ALU.mult))
                chain(nc.vector.scalar_tensor_tensor(out=t, in0=t, scalar=1.5, in1=y, op0=ALU.subtract, op1=ALU.mult))
                chain(nc.vector.scalar_tensor_tensor(out=h[:, q, :, :], in0=h[:, q, :, :], scalar=0.0,
                                                     in1=over_features(t), op0=ALU.min, op1=ALU.mult))
                for k in range(PARTS):
                    part = q * PARTS + k
                    if part >= 2:
                        dve.wait_ge(transposed, PB * (part - 1))
                    h_k = h[:, q, k * PT:(k + 1) * PT, :]
                    hi = hilo[:, part % 2, :, 0, :]
                    lo = hilo[:, part % 2, :, 1, :]
                    chain(nc.vector.tensor_single_scalar(hi.bitcast(i32), h_k.bitcast(i32), HI_MASK, ALU.bitwise_and))
                    nc.vector.tensor_tensor(lo, h_k, hi, ALU.subtract).then_inc(split, 1)

            centre(0)
            centre(1)
            half_variance(0)
            for q in range(NQ):
                if q + 2 < NQ:
                    centre(q + 2)
                if q + 1 < NQ:
                    half_variance(q + 1)
                normalise(q)

            def sum_columns(b, r, c, w, piece):
                a = adj_rows[:, r, c:c + w]
                return nc.vector.scalar_tensor_tensor(out=a, in0=a, scalar=1.0,
                                                      in1=gram[:, c // GC % 2, c % GC:c % GC + w],
                                                      op0=ALU.mult, op1=ALU.mult,
                                                      accum_out=partial[:, b, r, piece:piece + 1])

            def sum_row_tile(b, r):
                for g in range(NG):
                    if g * GC % HC == 0:
                        dve.wait_ge(adj_loaded[r][g * GC // HC], b * 16 + 16)
                    dve.wait_ge(gram_ready, b * GPB + (r * NG + g + 1))
                    sum_columns(b, r, g * GC, GC, g).then_inc(gram_used, 1)

            with dve.Fori(0, NB - 1) as b:
                for r in range(R):
                    sum_row_tile(b, r)
            for r in range(R - 1):
                sum_row_tile(NB - 1, r)
            for i, (c, w) in enumerate(LAST):
                dve.wait_ge(last_loaded[i], 16)
                dve.wait_ge(gram_ready, (NB - 1) * GPB + (R - 1) * NG + c // GC + 1)
                sum_columns(NB - 1, R - 1, c, w, i).then_inc(gram_used, 1)
            dve.wait_ge(gram_used, NB * GPB + len(LAST) - NG + 1)
            dve.wait_ge(out_ready, NB * R)
            y = base[:, NB - 1, (R - 1) * D:R * D]
            last_sum = partial[:, NB - 1, R - 1, len(LAST) - 1:len(LAST)].to_broadcast([P, D])
            nc.vector.scalar_tensor_tensor(out=y, in0=last_sum, scalar=-R_CONST, in1=y,
                                           op0=ALU.mult, op1=ALU.add).then_inc(last_ready, 1)

        @block.tensor
        def _(pe):
            def gram_group(b, r, g):
                if g == 0:
                    pe.wait_ge(weights_ready, b * R + (r + 1))
                for s in range(2):
                    for k in range(GB):
                        c = g * GC + k * BANK
                        ins = nc.tensor.matmul(gram[:, g % 2, k * BANK:(k + 1) * BANK], weights[:, r % 2, s, :],
                                               hT[:, c:c + BANK], start=(s == 0), stop=(s == 1))
                ins.then_inc(gram_ready, 1)

            def half_free(b, r, g):
                pe.wait_ge(gram_used, b * GPB + (r * NG + g))

            def rest_of_row_tile(b, r):
                for g in range(1, NG):
                    half_free(b, r, g)
                    gram_group(b, r, g)

            pe.wait_ge(ident_ready, 1)
            for n in range(NB):
                if n == (NQ - 1) * QB:
                    pe.wait_ge(gram_used, 1)
                    pe.wait_ge(hT_ready, GB)
                    gram_group(0, 0, 0)
                if n % PB == 0:
                    pe.wait_ge(split, n // PB + 1)
                if n >= GB:
                    pe.wait_ge(hT_ready, n - GB + 1)
                for r in range(R):
                    rows = hilo[:, n // PB % 2, n % PB * R + r, :, :].rearrange("p s d -> p (s d)")
                    ins = nc.tensor.transpose(bank(n)[:, r * P:(r + 1) * P], rows, ident[:, :])
                ins.then_inc(transposed, 1)
            pe.wait_ge(hT_ready, NB)
            with pe.Fori(0, NB - 1) as b:
                for r in range(R):
                    rest_of_row_tile(b, r)
                    if r + 1 < R:
                        half_free(b, r + 1, 0)
                        gram_group(b, r + 1, 0)
                    else:
                        half_free(b + 1, 0, 0)
                        gram_group(b + 1, 0, 0)
            for r in range(R):
                rest_of_row_tile(NB - 1, r)
                if r + 1 < R:
                    half_free(NB - 1, r + 1, 0)
                    gram_group(NB - 1, r + 1, 0)

        @block.scalar
        def _(act):
            def square(q):
                act.wait_ge(centred, q + 1)
                if q >= 2:
                    act.wait_ge(variance, q - 1)
                nc.scalar.activation(sq(q), h[:, q, :, :], ACT.Square).then_inc(squared, 1)

            def take_hT(q):
                for k in range(QB):
                    n = q * QB + k
                    act.wait_ge(transposed, n + 1)
                    src = bank(n).rearrange("k (r p) -> k p r", r=R)
                    dst = hT[:, n * BANK:(n + 1) * BANK].rearrange("k (p r) -> k p r", r=R)
                    nc.scalar.copy(dst, src).then_inc(hT_ready, 1)

            def lay_weights(b, r):
                rows = hT[:, :].rearrange("k (b p r) -> k b r p", r=R, p=P)
                nc.scalar.copy(weights[:, r % 2, 0, :], rows[:, b, r, :])
                nc.scalar.copy(weights[0:D, r % 2, 1, :], rows[D:2 * D, b, r, :])
                nc.scalar.copy(weights[D:2 * D, r % 2, 1, :], rows[0:D, b, r, :]).then_inc(weights_ready, 1)

            square(0)
            square(1)
            for q in range(NQ):
                act.wait_ge(variance, q + 1)
                nc.scalar.activation(std[:, q, :], half_var[:, q, :], ACT.Sqrt, scale=2.0).then_inc(std_ready, 1)
                if q + 2 < NQ:
                    square(q + 2)
                if q >= 1:
                    take_hT(q - 1)
                if q == 1:
                    act.wait_ge(hT_ready, 1)
                    lay_weights(0, 0)
            take_hT(NQ - 1)

            def finish(b, r, pieces=NG):
                act.wait_ge(gram_used, b * GPB + (r * NG + pieces + 1))
                nc.scalar.activation(unread[:, 0:pieces], partial[:, b, r, 0:pieces], ACT.Copy, scale=-R_CONST,
                                     accum_out=outer[:, r:r + 1]).then_inc(outer_ready, 1)
                act.wait_ge(outer_ready, b * R + (r + 1))
                y = base[:, b, r * D:(r + 1) * D]
                nc.scalar.activation(y, y, ACT.Identity, bias=outer[:, r:r + 1]).then_inc(out_ready, 1)

            def store(b, first=0, end=R):
                act.dma_start(out_v[:, b, first * D:end * D], base[:, b, first * D:end * D]).then_inc(stored, 16)

            act.wait_ge(hT_ready, NB)
            lay_weights(0, 1)
            for r in range(2, R):
                act.wait_ge(gram_ready, (r - 1) * NG)
                lay_weights(0, r)
                if r == 2:
                    act.wait_ge(base_ready, NQ)
                finish(0, r - 2)
            with act.Fori(1, NB) as b:
                for r in range(R):
                    act.wait_ge(gram_ready, b * GPB + (r - 1) * NG)
                    lay_weights(b, r)
                    if r < 2:
                        finish(b - 1, r + 2)
                    else:
                        finish(b, r - 2)
                    if r == 1:
                        act.wait_ge(out_ready, b * R)
                        store(b - 1)
            finish(NB - 1, 2)
            act.wait_ge(out_ready, NB * R - 1)
            store(NB - 1, end=R - 1)
            finish(NB - 1, 3, pieces=len(LAST) - 1)
            act.wait_ge(last_ready, 1)
            store(NB - 1, first=R - 1)
            act.wait_ge(stored, 16 * (NB + 1))


def kernel(x, adj, L0_gnn_t):
    import numpy as np
    import concourse.bacc as bacc
    from concourse.bass_utils import run_bass_kernel_spmd

    nc = bacc.Bacc("TRN2", target_bir_lowering=False, num_devices=1)
    arrays = {"x": np.ascontiguousarray(x), "adj": np.ascontiguousarray(adj)}
    ins = [nc.dram_tensor(name, a.shape, mybir.dt.from_np(a.dtype), kind="ExternalInput").ap()
           for name, a in arrays.items()]
    out = nc.dram_tensor("out", arrays["x"].shape, mybir.dt.float32, kind="ExternalOutput").ap()
    gnn_layer(nc, *ins, out)
    result = run_bass_kernel_spmd(nc, [arrays], core_ids=[0])
    return result.results[0]["out"]
```
